# Optimizing a Trainium2 kernel written in Bass

```python
import numpy as np
import jax
import jax.numpy as jnp

def _softmax(x, axis=-1):
    return jax.nn.softmax(x, axis=axis)

def _gelu(x):
    return jax.nn.gelu(x, approximate=True)

def _silu(x):
    return jax.nn.silu(x)

def _sigmoid(x):
    return jax.nn.sigmoid(x)

def _layernorm(x, axis=-1, eps=1e-05):
    m = jnp.mean(x, axis=axis, keepdims=True)
    v = jnp.var(x, axis=axis, keepdims=True)
    return (x - m) / jnp.sqrt(v + eps)

def _scatter_add(tgt, idx, src, axis=0):
    return tgt.at[idx].add(src)

def _segment_sum(src, seg, n):
    return jax.ops.segment_sum(src, seg, n)
kernel_name = 'mk_vit_tower_d2_tok_img768_r4_e685b1'

def setup_inputs(seed: int=0):
    np.random.seed(seed)
    _w = jnp.asarray

    def _rec_inputs():
        import jax
        import jax.numpy as jnp
        _rk = jax.random.key(seed)
        x = -4.65018e-05 + 0.999886 * jax.random.normal(jax.random.fold_in(_rk, 1), (16, 3, 96, 96), jnp.float32)
        return x
    x = _rec_inputs()

    def _L0_tok_setup():
        import jax, jax.numpy as jnp
        import numpy as np
        PATCH = 16
        EPS = 1e-05

        def _rms_norm(x, w):
            return x * jax.lax.rsqrt(jnp.mean(x * x, axis=-1, keepdims=True) + EPS) * w
        key = jax.random.key(seed)
        k1, k2 = jax.random.split(key)
        B, C, H, W = (64, 3, 128, 128)
        patch_dim = C * PATCH * PATCH
        dim = 192
        x = jax.random.normal(k1, (B, C, H, W), dtype=jnp.float32)
        bound = 1.0 / np.sqrt(patch_dim)
        W_proj = jax.random.uniform(k2, (dim, patch_dim), minval=-bound, maxval=bound, dtype=jnp.float32)
        b_proj = jnp.zeros((dim,), dtype=jnp.float32)
        g_in = jnp.ones((patch_dim,), dtype=jnp.float32)
        g_out = jnp.ones((dim,), dtype=jnp.float32)
        return {'x': x, 'W_proj': W_proj, 'b_proj': b_proj, 'g_in': g_in, 'g_out': g_out}
    _L0_tok_all = _L0_tok_setup()
    _L0_tok_in = {k: v for k, v in _L0_tok_all.items() if k in ('W_proj', 'b_proj', 'g_in', 'g_out')}
    del _L0_tok_all

    def _L0_attn_setup():
        import jax, jax.numpy as jnp
        import numpy as np
        D_MODEL = 192
        D_STATE = 16
        D_CONV = 4
        EXPAND = 2
        D_INNER = D_MODEL * EXPAND
        BATCH = 2
        SEQ = 1024
        key = jax.random.key(seed)
        ks = jax.random.split(key, 10)
        s = 0.02
        x = jax.random.normal(ks[0], (BATCH, SEQ, D_MODEL), dtype=jnp.float32)
        W_in = jax.random.normal(ks[1], (2 * D_INNER, D_MODEL), dtype=jnp.float32) * s
        W_conv = jax.random.normal(ks[2], (D_INNER, 1, D_CONV), dtype=jnp.float32) * s
        b_conv = jnp.zeros((D_INNER,), dtype=jnp.float32)
        W_dt = jax.random.normal(ks[3], (D_INNER, D_INNER), dtype=jnp.float32) * s
        b_dt = jnp.zeros((D_INNER,), dtype=jnp.float32)
        A_log = jnp.broadcast_to(jnp.log(jnp.arange(1, D_STATE + 1, dtype=jnp.float32))[None, :], (D_INNER, D_STATE)).copy()
        D_skip = jnp.ones((D_INNER,), dtype=jnp.float32)
        W_B = jax.random.normal(ks[4], (D_STATE, D_INNER), dtype=jnp.float32) * s
        W_C = jax.random.normal(ks[5], (D_STATE, D_INNER), dtype=jnp.float32) * s
        W_out = jax.random.normal(ks[6], (D_MODEL, D_INNER), dtype=jnp.float32) * s
        return {'x': x, 'W_in': W_in, 'W_conv': W_conv, 'b_conv': b_conv, 'W_dt': W_dt, 'b_dt': b_dt, 'A_log': A_log, 'D_skip': D_skip, 'W_B': W_B, 'W_C': W_C, 'W_out': W_out}
    _L0_attn_all = _L0_attn_setup()
    _L0_attn_in = {k: v for k, v in _L0_attn_all.items() if k in ('W_in', 'W_conv', 'b_conv', 'W_dt', 'b_dt', 'A_log', 'D_skip', 'W_B', 'W_C', 'W_out')}
    del _L0_attn_all

    def _L0_ffn_setup():
        import jax, jax.numpy as jnp
        import numpy as np
        S, B, DIM = (256, 4, 192)
        N_EXPERTS = 8
        HID = 512
        key = jax.random.key(seed)
        ks = jax.random.split(key, 6)
        scale = 0.02
        return {'hidden_states': jax.random.normal(ks[0], (S, B, DIM), dtype=jnp.float32), 'router_w': jax.random.normal(ks[1], (DIM, N_EXPERTS), dtype=jnp.float32) * scale, 'router_b': jnp.zeros((N_EXPERTS,), dtype=jnp.float32), 'w1': jax.random.normal(ks[2], (N_EXPERTS, DIM, HID), dtype=jnp.float32) * scale, 'w2': jax.random.normal(ks[3], (N_EXPERTS, DIM, HID), dtype=jnp.float32) * scale, 'w3': jax.random.normal(ks[4], (N_EXPERTS, HID, DIM), dtype=jnp.float32) * scale}
    _L0_ffn_all = _L0_ffn_setup()
    _L0_ffn_in = {k: v for k, v in _L0_ffn_all.items() if k in ('router_w', 'router_b', 'w1', 'w2', 'w3')}
    del _L0_ffn_all

    def _L1_attn_setup():
        import jax, jax.numpy as jnp
        import numpy as np
        N_HEAD = 12
        key = jax.random.key(seed)
        k1, k2, k3 = jax.random.split(key, 3)
        C = 192
        x = jax.random.normal(k1, (2, 1024, C), dtype=jnp.float32)
        w_qkv = jax.random.normal(k2, (C, 3 * C), dtype=jnp.float32) * C ** (-0.5)
        w_proj = jax.random.normal(k3, (C, C), dtype=jnp.float32) * C ** (-0.5)
        return {'x': x, 'w_qkv': w_qkv, 'w_proj': w_proj}
    _L1_attn_all = _L1_attn_setup()
    _L1_attn_in = {k: v for k, v in _L1_attn_all.items() if k in ('w_qkv', 'w_proj')}
    del _L1_attn_all

    def _L1_ffn_setup():
        import jax, jax.numpy as jnp
        import numpy as np
        D = 192
        I = 768
        E = 8
        K = 2
        LIMIT = 10.0
        VOCAB = 8192

        def _expert(xf, W1, W2, W3):
            gate = jnp.minimum(xf @ W1, LIMIT)
            up = jnp.clip(xf @ W3, -LIMIT, LIMIT)
            return jax.nn.silu(gate) * up @ W2
        key = jax.random.key(seed)
        ks = jax.random.split(key, 10)
        s = 0.02
        return {'x': jax.random.normal(ks[0], (1, 512, D), dtype=jnp.float32), 'input_ids': jax.random.randint(ks[1], (1, 512), 0, VOCAB, dtype=jnp.int64), 'gate_w': jax.random.normal(ks[2], (D, E), dtype=jnp.float32) * s, 'gate_bias': jnp.zeros((E,), dtype=jnp.float32), 'w1': jax.random.normal(ks[3], (E, D, I), dtype=jnp.float32) * s, 'w2': jax.random.normal(ks[4], (E, I, D), dtype=jnp.float32) * s, 'w3': jax.random.normal(ks[5], (E, D, I), dtype=jnp.float32) * s, 'w1s': jax.random.normal(ks[6], (D, I), dtype=jnp.float32) * s, 'w2s': jax.random.normal(ks[7], (I, D), dtype=jnp.float32) * s, 'w3s': jax.random.normal(ks[8], (D, I), dtype=jnp.float32) * s}
    _L1_ffn_all = _L1_ffn_setup()
    _L1_ffn_in = {k: v for k, v in _L1_ffn_all.items() if k in ('input_ids', 'gate_w', 'gate_bias', 'w1', 'w2', 'w3', 'w1s', 'w2s', 'w3s')}
    del _L1_ffn_all
    return {'x': x, 'L0_tok_W_proj': _L0_tok_in['W_proj'], 'L0_tok_b_proj': _L0_tok_in['b_proj'], 'L0_tok_g_in': _L0_tok_in['g_in'], 'L0_tok_g_out': _L0_tok_in['g_out'], 'L0_attn_W_in': _L0_attn_in['W_in'], 'L0_attn_W_conv': _L0_attn_in['W_conv'], 'L0_attn_b_conv': _L0_attn_in['b_conv'], 'L0_attn_W_dt': _L0_attn_in['W_dt'], 'L0_attn_b_dt': _L0_attn_in['b_dt'], 'L0_attn_A_log': _L0_attn_in['A_log'], 'L0_attn_D_skip': _L0_attn_in['D_skip'], 'L0_attn_W_B': _L0_attn_in['W_B'], 'L0_attn_W_C': _L0_attn_in['W_C'], 'L0_attn_W_out': _L0_attn_in['W_out'], 'L0_ffn_router_w': _L0_ffn_in['router_w'], 'L0_ffn_router_b': _L0_ffn_in['router_b'], 'L0_ffn_w1': _L0_ffn_in['w1'], 'L0_ffn_w2': _L0_ffn_in['w2'], 'L0_ffn_w3': _L0_ffn_in['w3'], 'L1_attn_w_qkv': _L1_attn_in['w_qkv'], 'L1_attn_w_proj': _L1_attn_in['w_proj'], 'L1_ffn_input_ids': _L1_ffn_in['input_ids'], 'L1_ffn_gate_w': _L1_ffn_in['gate_w'], 'L1_ffn_gate_bias': _L1_ffn_in['gate_bias'], 'L1_ffn_w1': _L1_ffn_in['w1'], 'L1_ffn_w2': _L1_ffn_in['w2'], 'L1_ffn_w3': _L1_ffn_in['w3'], 'L1_ffn_w1s': _L1_ffn_in['w1s'], 'L1_ffn_w2s': _L1_ffn_in['w2s'], 'L1_ffn_w3s': _L1_ffn_in['w3s']}

def reference(x, L0_tok_W_proj, L0_tok_b_proj, L0_tok_g_in, L0_tok_g_out, L0_attn_W_in, L0_attn_W_conv, L0_attn_b_conv, L0_attn_W_dt, L0_attn_b_dt, L0_attn_A_log, L0_attn_D_skip, L0_attn_W_B, L0_attn_W_C, L0_attn_W_out, L0_ffn_router_w, L0_ffn_router_b, L0_ffn_w1, L0_ffn_w2, L0_ffn_w3, L1_attn_w_qkv, L1_attn_w_proj, L1_ffn_input_ids, L1_ffn_gate_w, L1_ffn_gate_bias, L1_ffn_w1, L1_ffn_w2, L1_ffn_w3, L1_ffn_w1s, L1_ffn_w2s, L1_ffn_w3s):
    import jax
    import jax.numpy as jnp

    def _L0_tok_ref(x, W_proj, b_proj, g_in, g_out):
        import jax, jax.numpy as jnp
        import numpy as np
        PATCH = 16
        EPS = 1e-05

        def _rms_norm(x, w):
            return x * jax.lax.rsqrt(jnp.mean(x * x, axis=-1, keepdims=True) + EPS) * w
        B, C, H, W = x.shape
        p = PATCH
        h, w = (H // p, W // p)
        xr = x.reshape(B, C, h, p, w, p)
        xr = jnp.transpose(xr, (0, 2, 4, 3, 5, 1)).reshape(B, h * w, p * p * C)
        xn = _rms_norm(xr, g_in)
        y = jnp.einsum('bnd,ed->bne', xn, W_proj) + b_proj
        return _rms_norm(y, g_out)

    def _L0_attn_ref(x, W_in, W_conv, b_conv, W_dt, b_dt, A_log, D_skip, W_B, W_C, W_out):
        import jax, jax.numpy as jnp
        import numpy as np
        D_MODEL = 192
        D_STATE = 16
        D_CONV = 4
        EXPAND = 2
        D_INNER = D_MODEL * EXPAND
        BATCH = 2
        SEQ = 1024
        Bsz, T, _ = x.shape
        xz = x @ W_in.T
        x_ssm, z = jnp.split(xz, 2, axis=-1)
        xc = jnp.transpose(x_ssm, (0, 2, 1))
        xc = jax.lax.conv_general_dilated(xc, W_conv, window_strides=(1,), padding=[(D_CONV - 1, 0)], dimension_numbers=('NCH', 'OIH', 'NCH'), feature_group_count=D_INNER)
        xc = xc + b_conv[None, :, None]
        x_ssm = jax.nn.silu(jnp.transpose(xc, (0, 2, 1)))
        dt = jax.nn.softplus(x_ssm @ W_dt.T + b_dt)
        A = -jnp.exp(A_log)
        B_t = x_ssm @ W_B.T
        C_t = x_ssm @ W_C.T

        def step(state, inp):
            xt, dtt, bt, ct = inp
            dA = jnp.exp(dtt[:, :, None] * A[None])
            state = state * dA + (dtt * xt)[:, :, None] * bt[:, None, :]
            y_t = jnp.einsum('bds,bs->bd', state, ct)
            return (state, y_t)
        state0 = jnp.zeros((Bsz, D_INNER, D_STATE), dtype=x.dtype)
        xs = (jnp.transpose(x_ssm, (1, 0, 2)), jnp.transpose(dt, (1, 0, 2)), jnp.transpose(B_t, (1, 0, 2)), jnp.transpose(C_t, (1, 0, 2)))
        _, ys = jax.lax.scan(step, state0, xs)
        y = jnp.transpose(ys, (1, 0, 2))
        y = y + x_ssm * D_skip[None, None, :]
        y = y * jax.nn.silu(z)
        return y @ W_out.T

    def _L0_ffn_ref(hidden_states, router_w, router_b, w1, w2, w3):
        import jax, jax.numpy as jnp
        import numpy as np
        S, B, DIM = (256, 4, 192)
        N_EXPERTS = 8
        HID = 512
        s, b, h = hidden_states.shape
        route = jax.nn.softmax(hidden_states @ router_w + router_b, axis=2)
        max_prob = jnp.max(route, axis=2).reshape(-1, 1)
        max_ind = jnp.argmax(route, axis=2).reshape(-1)
        x = hidden_states.reshape(-1, h)
        out = jnp.zeros_like(x)
        for e in range(N_EXPERTS):
            mask = (max_ind == e)[:, None]
            xe = jnp.where(mask, x, 0.0)
            oe = jax.nn.silu(xe @ w1[e]) * (xe @ w2[e]) @ w3[e]
            out = out + jnp.where(mask, oe, 0.0)
        out = out.astype(jnp.bfloat16) * max_prob
        return out.reshape(s, b, h)

    def _L1_attn_ref(x, w_qkv, w_proj):
        import jax, jax.numpy as jnp
        import numpy as np
        N_HEAD = 12
        B, T, C = x.shape
        H = N_HEAD
        D = C // H
        qkv = x @ w_qkv
        q, k, v = jnp.split(qkv, 3, axis=-1)
        q = q.reshape(B, T, H, D).transpose(0, 2, 1, 3)
        k = k.reshape(B, T, H, D).transpose(0, 2, 1, 3)
        v = v.reshape(B, T, H, D).transpose(0, 2, 1, 3)
        scale = 1.0 / D ** 0.5
        att = jnp.einsum('bhqd,bhkd->bhqk', q, k) * scale
        att = jax.nn.softmax(att, axis=-1)
        y = jnp.einsum('bhqk,bhkd->bhqd', att, v)
        y = y.transpose(0, 2, 1, 3).reshape(B, T, C)
        return y @ w_proj

    def _L1_ffn_ref(x, input_ids, gate_w, gate_bias, w1, w2, w3, w1s, w2s, w3s):
        import jax, jax.numpy as jnp
        import numpy as np
        D = 192
        I = 768
        E = 8
        K = 2
        LIMIT = 10.0
        VOCAB = 8192

        def _expert(xf, W1, W2, W3):
            gate = jnp.minimum(xf @ W1, LIMIT)
            up = jnp.clip(xf @ W3, -LIMIT, LIMIT)
            return jax.nn.silu(gate) * up @ W2
        B, T, _ = x.shape
        flat = x.reshape(-1, D)
        N = flat.shape[0]
        scores = jnp.sqrt(jax.nn.softplus(flat @ gate_w))
        routed_scores = scores + gate_bias
        _, indices = jax.lax.top_k(routed_scores, K)
        weights = jnp.take_along_axis(scores, indices, axis=1)
        weights = weights / jnp.clip(weights.sum(axis=-1, keepdims=True), 1e-06)
        combine = jnp.zeros((N, E), dtype=weights.dtype)
        combine = combine.at[jnp.arange(N)[:, None], indices].add(weights)
        y = _expert(flat, w1s, w2s, w3s)
        gate_h = jnp.minimum(jnp.einsum('td,edi->eti', flat, w1), LIMIT)
        up_h = jnp.clip(jnp.einsum('td,edi->eti', flat, w3), -LIMIT, LIMIT)
        h = jax.nn.silu(gate_h) * up_h
        out_e = jnp.einsum('eti,eid->etd', h, w2)
        routed = jnp.einsum('etd,te->td', out_e, combine)
        return (y + routed).reshape(B, T, D)
    h = _L0_tok_ref(x, L0_tok_W_proj, L0_tok_b_proj, L0_tok_g_in, L0_tok_g_out)
    h = h + _L0_attn_ref(_layernorm(h, axis=-1), L0_attn_W_in, L0_attn_W_conv, L0_attn_b_conv, L0_attn_W_dt, L0_attn_b_dt, L0_attn_A_log, L0_attn_D_skip, L0_attn_W_B, L0_attn_W_C, L0_attn_W_out)
    h = h + _L0_ffn_ref(_layernorm(h, axis=-1), L0_ffn_router_w, L0_ffn_router_b, L0_ffn_w1, L0_ffn_w2, L0_ffn_w3)
    h = h + _L1_attn_ref(_layernorm(h, axis=-1), L1_attn_w_qkv, L1_attn_w_proj)
    h = h + _L1_ffn_ref(_layernorm(h, axis=-1), L1_ffn_input_ids, L1_ffn_gate_w, L1_ffn_gate_bias, L1_ffn_w1, L1_ffn_w2, L1_ffn_w3, L1_ffn_w1s, L1_ffn_w2s, L1_ffn_w3s)
    return h

_drawn_inputs = setup_inputs


def setup_inputs(seed=0):
    import zlib

    import numpy as np

    out = dict(_drawn_inputs(seed))
    spreads = {'L0_tok_b_proj': (0.0, 0.1),
     'L0_tok_g_in': (1.0, 0.2),
     'L0_tok_g_out': (1.0, 0.2),
     'L0_attn_b_conv': (0.0, 0.8),
     'L0_attn_b_dt': (0.0, 0.8),
     'L0_attn_D_skip': (1.0, 0.6),
     'L0_ffn_router_b': (0.0, 0.8),
     'L1_ffn_gate_bias': (0.0, 2.0)}
    factors = {'L0_attn_W_in': 8.0,
     'L0_attn_W_conv': 8.0,
     'L0_attn_W_dt': 8.0,
     'L0_attn_A_log': 8.0,
     'L0_attn_W_B': 8.0,
     'L0_attn_W_C': 8.0,
     'L0_attn_W_out': 8.0,
     'L0_ffn_router_w': 8.0,
     'L0_ffn_w1': 8.0,
     'L0_ffn_w2': 8.0,
     'L0_ffn_w3': 8.0,
     'L1_ffn_gate_w': 23.199,
     'L1_ffn_w1': 14.51,
     'L1_ffn_w2': 13.467,
     'L1_ffn_w3': 13.431,
     'L1_ffn_w1s': 21.764,
     'L1_ffn_w2s': 20.53,
     'L1_ffn_w3s': 20.413,
     'L1_attn_w_qkv': 8.0,
     'L1_attn_w_proj': 8.0}
    for name, (base, spread) in spreads.items():
        noise = np.random.default_rng([zlib.crc32(name.encode()), seed]).standard_normal(out[name].shape)
        drawn = base * np.exp(spread * noise) if base else spread * noise
        out[name] = jnp.asarray(drawn.astype(out[name].dtype))
    for name, factor in factors.items():
        out[name] = (out[name] * factor).astype(out[name].dtype)
    return out
```

```python
from contextlib import ExitStack

import concourse.bass as bass
import numpy as np
from concourse import mybir

ALU = mybir.AluOpType
ACT = mybir.ActivationFunctionType
F32 = mybir.dt.float32
BF16 = mybir.dt.bfloat16
AX_X = mybir.AxisListType.X
ds = bass.ds

B, CH, IMG, PATCH = 16, 3, 96, 16
SIDE = IMG // PATCH
S = SIDE * SIDE
T = B * S
PD = PATCH * PATCH * CH
D = 192
P = 128
TP = 96
NT = T // TP
KP, KC = 96, D // 96
HB = B // 2
TH = HB * S
PK = PD // P
DI = 2 * D
DC = DI // P
NS = 16
CONV = 4
E = 8
HID0, HID1 = 512, 768
NH, DH = 12, 16
GI = 3
GT = GI * S
NG = -(-B // GI)
HG = 4
HA = NH // HG
EPS = 1e-5
BIG = float(2.0 ** 100)
LIMIT = 10.0
SILU_LIMIT = LIMIT / (1.0 + float(np.exp(-LIMIT)))
EXP_SAFE = 30.0
QUAD = 4
NQ = NS // QUAD
UNITS = DC * 2 * NQ
TAB = "natural_log_exp_and_others"


def group_tokens(g):
    return min(GT, T - g * GT)


def build(nc, a, out):
    with ExitStack() as ctx:
        def sb(name, shape, dt=F32):
            return ctx.enter_context(nc.sbuf_tensor(name, shape, dt))

        sems = {}

        def sem(name):
            if name not in sems:
                sems[name] = ctx.enter_context(nc.semaphore(name))
            return sems[name]

        class Chain:

            def __init__(self, eng, name):
                self.eng, self.s, self.n = eng, sem(name), 0

            def __call__(self, ins, lag=0):
                self.n += 1
                ins.then_inc(self.s, 1)
                if self.n > lag:
                    self.eng.wait_ge(self.s, self.n - lag)

        ps = ctx.enter_context(nc.psum_tensor("ps", [P, 8, 512], F32))

        ident = sb("ident", [P, P])
        h = sb("h", [TP, NT, D])
        xn = sb("xn", [TP, NT, D])
        xnT = sb("xnT", [KP, KC, T])
        bn = sb("bn", [TP, NT, 6])
        mv = sb("mv", [TP, NT, 2])
        lnv = sb("lnv", [TP, NT])
        rstd = sb("rstd", [TP, NT])
        eps_tile = sb("eps", [TP, 1])

        arena = sb("arena", [P, 11 * QUAD * TH + DC * T])
        xT = arena[:, 0:PK * T].rearrange("p (k t) -> p k t", k=PK)
        xtok = arena[0:TP, PK * T:PK * T + NT * PD].rearrange("p (n d) -> p n d", n=NT)
        wp = sb("wp", [P, PK, D])
        gin = sb("gin", [P, PK])
        bproj = sb("bproj", [TP, D])
        gout = sb("gout", [TP, D])
        ssq = sb("ssq", [TP, 4, NT])

        win = sb("win", [KP, KC, 2 * DI])
        wconv = sb("wconv", [P, DC, CONV])
        bconv = sb("bconv", [P, DC])
        wdt = sb("wdt", [P, DC, DI])
        bdt = sb("bdt", [P, DC])
        negA = sb("negA", [P, DC, NS])
        dskip = sb("dskip", [P, DC])
        wbc = sb("wbc", [P, DC, 96])
        wout = sb("wout", [P, DC, D])
        sel = sb("sel", [96, 32, P], BF16)
        U = QUAD * TH
        rings = arena[:, 0:11 * U].rearrange("p (r q t) -> p r q t", r=11, q=QUAD)
        dA, dBx, hs, prod = rings[:, 0:3], rings[:, 3:5], rings[:, 5:8], rings[:, 8:11]
        xpad = sb("xpad", [P, DC, B, S + CONV - 1])
        cacc = sb("cacc", [P, DC, T])
        xczs = sb("xczs", [P, 2 * DC * T])
        xc = xczs[:, 0:DC * T].rearrange("p (c t) -> p c t", c=DC)
        zs = xczs[:, DC * T:].rearrange("p (c t) -> p c t", c=DC)
        dtb = sb("dtb", [P, DC, T])
        dtx = arena[:, 11 * U:11 * U + DC * T].rearrange("p (c t) -> p c t", c=DC)
        yz = cacc
        Cb = sb("Cb", [P, NS, T])
        junk = Cb[0:TP, :, :].rearrange("p a b -> p (a b)")[:, 0:2 * PD].rearrange("p (r d) -> p r d", r=2)
        bcp = sb("bcp", [96, T], BF16)
        bcm = sb("bcm", [96, T], BF16)
        bcr = sb("bcr", [96, T])

        o = 0

        def carve(cols, where=arena, rows=P):
            nonlocal o
            o += cols
            return where[0:rows, o - cols:o]

        wqk = carve(KC * 2 * HA * P, xczs, KP).rearrange("p (k m) -> p k m", k=KC)
        wv = carve(KC * D, xczs, KP).rearrange("p (k m) -> p k m", k=KC)
        wpr = carve(KC * D, xczs, KP).rearrange("p (k m) -> p k m", k=KC)
        qmask = carve(T, xczs)
        kmask = carve(T, xczs)
        o = 0

        qT = carve(HA * T).rearrange("p (a t) -> p a t", a=HA)
        kT = carve(HA * T).rearrange("p (a t) -> p a t", a=HA)
        vaug = carve(NG * NH * (DH + 1)).rearrange("p (g h d) -> p g h d", g=NG, h=NH)
        zm = carve(NG * HA * P).rearrange("p (g a m) -> p g a m", g=NG, a=HA)
        pT = carve(2 * 2 * HA * GT).rearrange("p (r j f) -> p r j f", r=2, j=2)
        yat = carve(2 * D).rearrange("p (r d) -> p r d", r=2)
        rden = carve(2 * NH).rearrange("p (r d) -> p r d", r=2)
        yT = carve(KC * T).rearrange("p (k t) -> p k t", k=KC)

        wgu = sb("wgu", [KP, 2, KC, 2 * HID1])
        wdn = sb("wdn", [P, 2, HID1 // P, D])
        hT = Cb[:, :, :].rearrange("p a b -> p (a b)")[:, 0:HID1 // P * 2 * T].rearrange(
            "p (r m t) -> p r m t", r=2, m=HID1 // P)
        up = arena[:, 0:2 * TH].rearrange("p (r t) -> p r t", r=2)
        gs = arena[:, 2 * TH:4 * TH].rearrange("p (r t) -> p r t", r=2)
        acc = xpad[0:TP].rearrange("p c b t -> p (c b t)")[:, 0:NT * D].rearrange("p (n d) -> p n d", n=NT)
        spare = Cb[0:TP].rearrange("p a b -> p (a b)")[:, HID1 // P * 2 * T:]
        accb = spare[:, 0:NT * D // 2].bitcast(BF16).rearrange("p (n d) -> p n d", n=NT)
        wr = sb("wr", [KP, 2, KC, E])
        rb = sb("rb", [TP, 2, E])
        first = sb("first", [TP, E])
        rt = spare[:, NT * D // 2:NT * D // 2 + 12 * NT * E].rearrange("p (r n e) -> p r n e", r=12, n=NT)
        rs = sb("rs", [TP, 4, NT])
        cw = sb("cw", [TP, E + 1, NT])
        mp = sb("mp", [TP, NT])

        block = ctx.enter_context(nc.Block())
        hid = (HID0, HID1)
        nexp = (E, E + 1)
        wgu_d, wdn_d = (a["gu0"], a["gu1"]), (a["dn0"], a["dn1"])

        def half(ap, n):
            return ap[:, n * TH:(n + 1) * TH]

        @block.sync
        def _(sp):
            def load(dst, name, key=None):
                sp.dma_start(dst, a[name]).then_inc(sem("ld_" + (key or name)), 16)

            load(wp[:], "wp")
            load(gin[:], "gin")
            for n in range(2):
                sp.dma_start(xT[:, :, n * TH:(n + 1) * TH], a["xT"][:, :, n * TH:(n + 1) * TH]).then_inc(
                    sem(f"ld_xT{n}"), 16)
            load(win[:], "win")
            load(wconv[:], "wconv", "small")
            load(bconv[:], "bconv", "small")
            load(bdt[:], "bdt", "small")
            load(negA[:], "alog", "small")
            load(dskip[:], "dskip", "small")
            load(wbc[:], "wbc", "proj")
            load(wdt[:], "wdt", "proj")
            load(sel[:], "sel", "proj")
            load(wout[:], "wout", "proj")

            def load_expert(layer, e, slot, w=None, users=None):
                m = hid[layer]
                if w is not None:
                    sp.wait_ge(sem(f"down_mm{layer if users is None else users}"), w)
                src = wgu_d[layer][e] if isinstance(e, int) else wgu_d[layer][ds(e, 1)].rearrange("o p k m -> p (o k) m")
                dn = wdn_d[layer][e] if isinstance(e, int) else wdn_d[layer][ds(e, 1)].rearrange("o p k m -> p (o k) m")
                sp.dma_start(wgu[:, slot, :, 0:2 * m], src).then_inc(sem(f"ld_exp{layer}_{slot}"), 16)
                sp.dma_start(wdn[:, slot, 0:m // P, :], dn).then_inc(sem(f"ld_exp{layer}_{slot}"), 16)

            load_expert(0, 0, 0)
            load_expert(0, 1, 1)
            load(wr[:], "wr")
            load(rb[:], "rb", "wr")
            load(first[:], "first", "wr")
            sp.wait_ge(sem("yz_ready"), 2 * DC)
            load(wqk, "wqk", "attn")
            load(wv, "wv", "attn")
            load(wpr, "wpr", "attn")
            load(qmask, "qmask", "attn")
            load(kmask, "kmask", "attn")
            with sp.Fori(1, E // 2) as i:
                load_expert(0, 2 * i, 0, 3 * (2 * i - 1))
                load_expert(0, 2 * i + 1, 1, 3 * (2 * i))
            load_expert(1, 0, 0, 3 * (E - 1), users=0)
            load_expert(1, 1, 1, 3 * E, users=0)
            with sp.Fori(1, E // 2) as i:
                load_expert(1, 2 * i, 0, 3 * (2 * i - 1))
                load_expert(1, 2 * i + 1, 1, 3 * (2 * i))
            load_expert(1, E, 0, 3 * (E - 1))
            for i in range(NT):
                sp.wait_ge(sem("h_final"), i + 1)
                sp.dma_start(out[i * TP:(i + 1) * TP, :], h[:, i, :]).then_inc(sem("stored"), 16)
            sp.wait_ge(sem("stored"), 16 * NT)

        @block.tensor
        def _(pe):
            def mm(o_, l, r, start, stop):
                return nc.tensor.matmul(o_, l, r, start=start, stop=stop)

            def transposes(src, L):
                if L == 0:
                    pe.wait_ge(sem("ld_ident"), 16)
                for i in range(NT):
                    pe.wait_ge(sem(f"ln_xn{L}"), i + 1)
                    n, j = i // (NT // 2), i % (NT // 2)
                    for k in range(KC):
                        last = nc.tensor.transpose(ps[0:KP, 2 * n + k, j * TP:(j + 1) * TP],
                                                   src[:, i, k * KP:(k + 1) * KP], ident[0:TP, 0:TP])
                    if j == NT // 2 - 1:
                        last.then_inc(sem(f"ln_tr{L}"), 1)

            pe.wait_ge(sem("wg_ready"), 1)
            for i in range(NT):
                if i % (NT // 2) == 0:
                    pe.wait_ge(sem(f"ld_xT{i // (NT // 2)}"), 16)
                for k in range(PK):
                    last = mm(ps[0:TP, i, 0:D], xT[:, k, i * TP:(i + 1) * TP], wp[:, k, :], k == 0, k == PK - 1)
                last.then_inc(sem("tok_mm"), 1)

            pe.wait_ge(sem("tok_y"), NT)
            transposes(xn, 0)
            pe.wait_ge(sem("ld_win"), 16)
            pe.wait_ge(sem("ln_xnT0"), 2)
            for n in range(4 * DC):
                if 4 <= n < 4 + 2 * DC:
                    pe.wait_ge(sem("in_x"), n - 3)
                elif n >= 4 + 2 * DC:
                    pe.wait_ge(sem("in_z"), n - 3 - 2 * DC)
                m, hf = n // 2, n % 2
                for k in range(KC):
                    last = mm(ps[:, 4 + n % 4, 0:TH], win[:, k, m * P:(m + 1) * P], half(xnT[:, k, :], hf),
                              k == 0, k == KC - 1)
                last.then_inc(sem("in_mm"), 1)
            pe.wait_ge(sem("xc_ready"), DC)
            pe.wait_ge(sem("ld_proj"), 64)
            for hf in range(2):
                for k in range(DC):
                    last = mm(ps[0:96, hf, 0:TH], wbc[:, k, :], half(xc[:, k, :], hf), k == 0, k == DC - 1)
                last.then_inc(sem("bc_mm"), 1)
            for n in range(2 * DC):
                m, hf = n // 2, n % 2
                for k in range(DC):
                    last = mm(ps[:, 2 + n, 0:TH], wdt[:, k, m * P:(m + 1) * P], half(xc[:, k, :], hf),
                              k == 0, k == DC - 1)
                last.then_inc(sem("dt_mm"), 1)
            pe.wait_ge(sem("bc_split"), 1)
            pe.wait_ge(sem("dt_ready"), DC)

            def spread(bank, row, hf):
                return mm(ps[:, bank, 0:TH], sel[:, row, :], half(bcp, hf), True, True)

            def spread_b(u):
                hf, q = u // NQ % 2, u % NQ
                for v in (2 * u, 2 * u + 1):
                    if v >= 2:
                        pe.wait_ge(sem("dbx_done"), v - 1)
                    for j in range(2):
                        last = spread(2 * (v % 2) + j, q * QUAD + 2 * (v % 2) + j, hf)
                    last.then_inc(sem("b_mm"), 1)

            def spread_c(s):
                if s >= 1:
                    pe.wait_ge(sem("cb_ready"), s)
                for hf in range(2):
                    last = spread(4 + hf, NS + s, hf)
                last.then_inc(sem("c_mm"), 1)

            def sum_states(u):
                g, q = u // NQ, u % NQ
                pe.wait_ge(sem("prod_done"), u + 1)
                if g >= 2 and q == 0:
                    pe.wait_ge(sem("y_evac"), g - 1)
                for j in range(QUAD):
                    last = mm(ps[:, 6 + g % 2, 0:TH], ident[:, :], prod[:, u % 3, j, :],
                              q == 0 and j == 0, q == NQ - 1 and j == QUAD - 1)
                last.then_inc(sem("y_mm"), 1)

            LAG = 3
            for u in range(UNITS + LAG):
                if u < UNITS:
                    spread_b(u)
                if u < NQ:
                    for s in range(u * QUAD, (u + 1) * QUAD):
                        spread_c(s)
                if u >= LAG:
                    sum_states(u - LAG)
            pe.wait_ge(sem("yz_ready"), 2 * DC)
            pe.wait_ge(sem("dbx_done"), 2 * UNITS)
            for i in range(NT):
                for c in range(DC):
                    last = mm(ps[0:TP, i, 0:D], yz[:, c, i * TP:(i + 1) * TP], wout[:, c, :], c == 0, c == DC - 1)
                last.then_inc(sem("mo_mm"), 1)

            def experts(L):
                H = hid[L]
                M = H // P
                unit, down = sem(f"gu_mm{L}"), sem(f"down_mm{L}")
                pe.wait_ge(sem("ld_wr"), 48)
                pe.wait_ge(sem(f"ln_xnT{2 * L + 1}"), 2)
                for i in range(NT):
                    for k in range(KC):
                        last = mm(ps[0:TP, 7, i * E:(i + 1) * E], xnT[:, k, i * TP:(i + 1) * TP], wr[:, L, k, :],
                                  k == 0, k == KC - 1)
                last.then_inc(sem(f"route_mm{L}"), 1)

                def gate_up(e, slot, loaded):
                    pe.wait_ge(sem(f"ld_exp{L}_{slot}"), loaded)
                    for n in range(2 * M):
                        m, hf = n // 2, n % 2
                        if not (isinstance(e, int) and e == 0 and n < 2):
                            pe.wait_ge(sem(f"h_done{L}"), e * (2 * M) + n - 1)
                        for part in range(2):
                            for k in range(KC):
                                last = mm(ps[:, 2 * (n % 2) + part, 0:TH],
                                          wgu[:, slot, k, part * H + m * P:part * H + (m + 1) * P],
                                          half(xnT[:, k, :], hf), k == 0, k == KC - 1)
                        last.then_inc(unit, 1)
                        if n == 2 and not (isinstance(e, int) and e == 0):
                            down_proj(e - 1, 1 - slot)

                def down_proj(e, slot):
                    pe.wait_ge(sem(f"h_done{L}"), (e + 1) * (2 * M))
                    for b in range(NT // 2):
                        if not (isinstance(e, int) and e == 0):
                            pe.wait_ge(sem(f"comb_done{L}"), e * (NT // 2) - (NT // 2 - 1) + b)
                        for i in (2 * b, 2 * b + 1):
                            for m in range(M):
                                last = mm(ps[0:TP, 4 + b, (i % 2) * D:(i % 2 + 1) * D],
                                          hT[:, slot, m, i * TP:(i + 1) * TP], wdn[:, slot, m, :],
                                          m == 0, m == M - 1)
                        last.then_inc(down, 1)

                gate_up(0, 0, 32)
                gate_up(1, 1, 32)
                with pe.Fori(1, E // 2) as i:
                    gate_up(2 * i, 0, 32 * i + 32)
                    gate_up(2 * i + 1, 1, 32 * i + 32)
                if L == 1:
                    gate_up(E, 0, 32 * (E // 2 + 1))
                down_proj(nexp[L] - 1, (nexp[L] - 1) % 2)

            transposes(xn, 1)
            experts(0)

            transposes(xn, 2)
            pe.wait_ge(sem("ld_attn"), 80)
            pe.wait_ge(sem("ln_xnT2"), 2)
            for n in range(4 * HA):
                m, hf = n // 2, n % 2
                if n >= 4:
                    pe.wait_ge(sem("qk_done"), n - 3)
                for k in range(KC):
                    last = mm(ps[:, 4 + n % 4, 0:TH], wqk[:, k, m * P:(m + 1) * P], half(xnT[:, k, :], hf),
                              k == 0, k == KC - 1)
                last.then_inc(sem("qk_mm"), 1)
            for g in range(NG):
                G = group_tokens(g)
                if g >= 4:
                    pe.wait_ge(sem("v_done"), g - 3)
                for k in range(KC):
                    last = mm(ps[0:G, g % 4, 0:D], xnT[:, k, g * GT:g * GT + G], wv[:, k, :], k == 0, k == KC - 1)
                last.then_inc(sem("v_mm"), 1)

            def pairs():
                return [(g, jj) for g in range(NG) for jj in range(2)]

            def scores(left, right, rows, g, jj, bank):
                G = group_tokens(g)
                c = slice(g * GT, g * GT + G)
                for aa in range(HA):
                    for j in (2 * jj, 2 * jj + 1):
                        last = mm(ps[0:G, bank + j % 2, aa * GT:aa * GT + G],
                                  left[32 * j:32 * j + rows, aa, c], right[32 * j:32 * j + rows, aa, c], True, True)
                return last

            pe.wait_ge(sem("qk_done"), 4 * HA)
            pe.wait_ge(sem("v_done"), NG)
            for n, (g, jj) in enumerate(pairs()):
                if n >= 4:
                    pe.wait_ge(sem("max_done"), n - 3)
                scores(qT, kT, DH + GI, g, jj, 2 * (n % 4)).then_inc(sem("s_mm"), 1)
            for g in range(NG):
                G = group_tokens(g)
                pe.wait_ge(sem("max_done"), 2 * NG)
                if g >= 2:
                    pe.wait_ge(sem("qm_done"), g - 1)
                for aa in range(HA):
                    last = mm(ps[:, 6 + g % 2, aa * GT:aa * GT + G], zm[0:G, g, aa, :], ident[0:G, 0:G], True, True)
                last.then_inc(sem("zm_mm"), 1)
            pe.wait_ge(sem("qm_done"), NG)

            def weighted(n, g, jj):
                G = group_tokens(g)
                pe.wait_ge(sem("p_done"), n + 1)
                if jj == 0 and g >= 1:
                    pe.wait_ge(sem("yat_done"), g)
                for aa in range(HA):
                    for j in (2 * jj, 2 * jj + 1):
                        hd = HG * aa + j
                        last = mm(ps[0:G, 6, hd * (DH + 1):(hd + 1) * (DH + 1)],
                                  pT[0:G, n % 2, j % 2, aa * G:(aa + 1) * G], vaug[0:G, g, hd, :], True, True)
                last.then_inc(sem("pv_mm"), 1)

            def turn(g):
                G = group_tokens(g)
                pe.wait_ge(sem("yat_done"), g + 1)
                if g >= 1:
                    pe.wait_ge(sem("yT_done"), g)
                for k in range(KC):
                    last = nc.tensor.transpose(ps[0:KP, 7, k * P:k * P + G], yat[0:G, g % 2, k * KP:(k + 1) * KP],
                                               ident[0:G, 0:G])
                last.then_inc(sem("yT_tr"), 1)

            pr = pairs()
            for n in range(len(pr) + 3):
                if n < len(pr):
                    g, jj = pr[n]
                    if n >= 3:
                        pe.wait_ge(sem("p_done"), n - 2)
                    scores(kT, qT, DH + GI + 1, g, jj, 2 * (n % 3)).then_inc(sem("st_mm"), 1)
                if 1 <= n <= len(pr):
                    weighted(n - 1, *pr[n - 1])
                if n >= 3 and (n - 3) % 2 == 0 and (n - 3) // 2 < NG:
                    turn((n - 3) // 2)
            pe.wait_ge(sem("yT_done"), NG)
            for i in range(NT):
                for k in range(KC):
                    last = mm(ps[0:TP, i, 0:D], yT[0:KP, k, i * TP:(i + 1) * TP], wpr[:, k, :], k == 0, k == KC - 1)
                last.then_inc(sem("ao_mm"), 1)

            transposes(xn, 3)
            experts(1)

        @block.scalar
        def _(act):
            link = Chain(act, "act_chain")

            def load(dst, name, key=None):
                act.dma_start(dst, a[name]).then_inc(sem("ld_" + (key or name)), 16)

            load(xtok, "xtok")
            load(bproj[:], "bproj", "tokv")
            load(gout[:], "gout", "tokv")
            load(ident[:], "ident")
            act.preload_act_table_set(TAB)

            def rsqrt(dst, src, tmp, scale):
                link(nc.scalar.activation(tmp, src, ACT.Ln, bias=eps_tile[:, 0:1], scale=scale))
                return nc.scalar.activation(dst, tmp, ACT.Exp, scale=-0.5)

            act.wait_ge(sem("consts"), 1)
            act.wait_ge(sem("ld_xtok"), 16)
            for i in range(NT):
                link(nc.scalar.activation(junk[:, i % 2, :], xtok[:, i, :], ACT.Square,
                                          accum_out=ssq[:, 0, i:i + 1]), 1 if i < NT - 1 else 0)
            rsqrt(ssq[:, 1, :], ssq[:, 0, :], lnv[:], 1.0 / PD).then_inc(sem("r_in"), 1)
            for i in range(NT):
                act.wait_ge(sem("tok_y"), i + 1)
                link(nc.scalar.activation(junk[:, i % 2, 0:D], h[:, i, :], ACT.Square,
                                          accum_out=ssq[:, 2, i:i + 1]), 1 if i < NT - 1 else 0)
            rsqrt(ssq[:, 3, :], ssq[:, 2, :], lnv[:], 1.0 / D).then_inc(sem("r_out"), 1)

            def norm(L, done):
                act.wait_ge(sem(f"ln_var{L}"), 1)
                rsqrt(rstd[:], mv[:, :, 1], lnv[:], 1.0).then_inc(sem(f"ln_rstd{L}"), 1)
                for n in range(2):
                    act.wait_ge(sem(f"ln_tr{L}"), n + 1)
                    nc.scalar.activation(xnT[:, :, n * TH:(n + 1) * TH], ps[0:KP, 2 * n:2 * n + KC, 0:TH],
                                         ACT.Copy).then_inc(sem(done), 1)

            norm(0, "ln_xnT0")
            for n in range(2 * DC):
                c, hf = n // 2, n % 2
                act.wait_ge(sem("in_mm"), 2 * DC + n + 1)
                nc.scalar.activation(half(zs[:, c, :], hf), ps[:, 4 + (2 * DC + n) % 4, 0:TH],
                                     ACT.Silu).then_inc(sem("in_z"), 1)
            for c in range(DC):
                act.wait_ge(sem("conv_done"), c + 1)
                nc.scalar.activation(xc[:, c, :], cacc[:, c, :], ACT.Silu).then_inc(sem("xc_ready"), 1)
            act.preload_act_table_set(TAB)
            act.wait_ge(sem("ld_small"), 80)
            link(nc.scalar.activation(negA[:, :, :], negA[:, :, :], ACT.Exp))
            link(nc.scalar.activation(negA[:, :, :], negA[:, :, :], ACT.Copy, scale=-1.0))
            for c in range(DC):
                act.wait_ge(sem("dt_min"), c + 1)
                link(nc.scalar.activation(dtb[:, c, :], dtb[:, c, :], ACT.Exp))
                nc.scalar.activation(dtb[:, c, :], dtb[:, c, :], ACT.Ln, bias=1.0).then_inc(sem("dt_ln"), 1)

            act.wait_ge(sem("rings_clear"), 1)
            for u in range(UNITS):
                c, hf, q = u // (2 * NQ), u // NQ % 2, u % NQ
                if q == 0 and hf == 0:
                    act.wait_ge(sem("dt_ready"), c + 1)
                if u >= 3:
                    act.wait_ge(sem("scan_done"), u - 2)
                for j in range(QUAD):
                    s = q * QUAD + j
                    last = nc.scalar.activation(
                        dA[:, u % 3, j, :].rearrange("p (b t) -> p b t", b=HB)[:, :, 1:S],
                        half(dtb[:, c, :], hf).rearrange("p (b t) -> p b t", b=HB)[:, :, 1:S],
                        ACT.Exp, scale=negA[:, c, s:s + 1])
                last.then_inc(sem("dA_ready"), 1)
                if u < NQ:
                    for s in range(u * QUAD, (u + 1) * QUAD):
                        act.wait_ge(sem("c_mm"), s + 1)
                        nc.scalar.activation(Cb[:, s, :].rearrange("p (n t) -> p n t", n=2), ps[:, 4:6, 0:TH],
                                             ACT.Copy).then_inc(sem("cb_ready"), 1)

            def experts(L):
                M = hid[L] // P

                def silus(e):
                    for n in range(2 * M):
                        act.wait_ge(sem(f"gu_mm{L}"), e * (2 * M) + n + 1)
                        if not (isinstance(e, int) and e == 0 and n < 2):
                            act.wait_ge(sem(f"h_done{L}"), e * (2 * M) + n - 1)
                        nc.scalar.activation(gs[:, n % 2, :], ps[:, 2 * (n % 2), 0:TH],
                                             ACT.Silu).then_inc(sem(f"silu_done{L}"), 1)

                silus(0)
                with act.Fori(1, nexp[L]) as e:
                    silus(e)

            norm(1, "ln_xnT1")
            act.wait_ge(sem("route_x0"), 1)
            nc.scalar.activation(rt[:, 1], rt[:, 0], ACT.Exp).then_inc(sem("route_exp0"), 1)
            experts(0)
            act.preload_act_table_set(TAB)

            norm(2, "ln_xnT2")
            for g in range(NG):
                G = group_tokens(g)
                act.wait_ge(sem("v_mm"), g + 1)
                nc.scalar.activation(vaug[0:G, g, :, 0:DH], ps[0:G, g % 4, 0:D].rearrange("p (h d) -> p h d", h=NH),
                                     ACT.Copy).then_inc(sem("v_done"), 1)
            for n in range(2 * NG):
                G = group_tokens(n // 2)
                act.wait_ge(sem("st_mm"), n + 1)
                if n >= 2:
                    act.wait_ge(sem("pv_mm"), n - 1)
                bank = 2 * (n % 3)
                nc.scalar.activation(pT[0:G, n % 2, :, 0:HA * G].rearrange("p j (a t) -> p j a t", a=HA),
                                     ps[0:G, bank:bank + 2, 0:HA * GT].rearrange("p j (a t) -> p j a t", a=HA)[:, :, :, 0:G],
                                     ACT.Exp).then_inc(sem("p_done"), 1)

            norm(3, "ln_xnT3")
            act.wait_ge(sem("route_x1"), 1)
            nc.scalar.activation(rt[:, 1], rt[:, 0], ACT.Exp).then_inc(sem("route_exp1"), 1)
            act.wait_ge(sem("route_u1"), 1)
            nc.scalar.activation(rt[:, 3], rt[:, 2], ACT.Ln).then_inc(sem("route_ln1"), 1)
            act.wait_ge(sem("route_sp1"), 1)
            nc.scalar.activation(rt[:, 5], rt[:, 4], ACT.Sqrt).then_inc(sem("route_sqrt1"), 1)
            experts(1)

        @block.gpsimd
        def _(pool):
            nc.gpsimd.memset(xpad[:, :, :, 0:CONV - 1], 0.0).then_inc(sem("pads_clear"), 1)
            pool.wait_ge(sem("tok_mm"), NT)
            pool.wait_ge(sem("r_in"), 1)
            dA0 = arena[:, 0:3 * U].rearrange("p (b t) -> p b t", t=S)
            nc.gpsimd.memset(dA0[:, :, 0:1], 0.0).then_inc(sem("rings_clear"), 1)
            for u in range(UNITS):
                hf, q = u // NQ % 2, u % NQ
                pool.wait_ge(sem("scan_done"), u + 1)
                if u < NQ:
                    pool.wait_ge(sem("cb_ready"), (u + 1) * QUAD)
                if u >= 3:
                    pool.wait_ge(sem("y_mm"), u - 2)
                nc.gpsimd.tensor_tensor(prod[:, u % 3], hs[:, u % 3],
                                        Cb[:, q * QUAD:(q + 1) * QUAD, hf * TH:(hf + 1) * TH],
                                        ALU.mult).then_inc(sem("prod_done"), 1)
            pool.wait_ge(sem("mo_mm"), NT)
            nc.gpsimd.memset(vaug[:, :, :, DH:DH + 1], 1.0)
            nc.gpsimd.memset(zm[:], 0.0).then_inc(sem("attn_consts"), 1)

        @block.vector
        def _(dve):
            link = Chain(dve, "dve_chain")
            V = nc.vector
            V.memset(eps_tile[:], EPS).then_inc(sem("consts"), 1)
            dve.wait_ge(sem("ld_wp"), 16)
            dve.wait_ge(sem("ld_gin"), 16)
            for k in range(PK):
                last = V.tensor_scalar(wp[:, k, :], wp[:, k, :], gin[:, k:k + 1], None, ALU.mult)
            last.then_inc(sem("wg_ready"), 1)
            dve.wait_ge(sem("r_in"), 1)
            dve.wait_ge(sem("ld_tokv"), 32)
            for i in range(NT):
                dve.wait_ge(sem("tok_mm"), i + 1)
                V.scalar_tensor_tensor(h[:, i, :], ps[0:TP, i, 0:D], ssq[:, 1, i:i + 1], bproj[:], ALU.mult,
                                       ALU.add).then_inc(sem("tok_y"), 1)
            dve.wait_ge(sem("r_out"), 1)
            for i in range(NT):
                last = V.scalar_tensor_tensor(h[:, i, :], h[:, i, :], ssq[:, 3, i:i + 1], gout[:], ALU.mult, ALU.mult)
            link(last)

            def norm(L):
                for i in range(NT):
                    last = V.bn_stats(bn[:, i, :], h[:, i, :])
                link(last)
                for i in range(NT):
                    last = V.bn_aggr(mv[:, i, :], bn[:, i, :])
                last.then_inc(sem(f"ln_var{L}"), 1)
                dve.wait_ge(sem(f"ln_rstd{L}"), 1)
                for i in range(NT):
                    V.tensor_scalar(xn[:, i, :], h[:, i, :], mv[:, i, 0:1], rstd[:, i:i + 1], ALU.subtract,
                                    ALU.mult).then_inc(sem(f"ln_xn{L}"), 1)

            norm(0)
            dve.wait_ge(sem("pads_clear"), 1)
            for n in range(2 * DC):
                c, hf = n // 2, n % 2
                dve.wait_ge(sem("in_mm"), n + 1)
                V.tensor_copy(xpad[:, c, hf * HB:(hf + 1) * HB, CONV - 1:],
                              ps[:, 4 + n % 4, 0:TH].rearrange("p (b t) -> p b t", b=HB)).then_inc(sem("in_x"), 1)
            dve.wait_ge(sem("ld_small"), 80)
            dve.wait_ge(sem("in_x"), 2 * DC)
            cv = [cacc[:, c, :].rearrange("p (b t) -> p b t", b=B) for c in range(DC)]
            for j in range(CONV):
                for c in range(DC):
                    tap = xpad[:, c, :, j:j + S]
                    if j == 0:
                        last = V.tensor_scalar(cv[c], tap, wconv[:, c, 0:1], bconv[:, c:c + 1], ALU.mult, ALU.add)
                    else:
                        last = V.scalar_tensor_tensor(cv[c], tap, wconv[:, c, j:j + 1], cv[c], ALU.mult, ALU.add)
                    if j == CONV - 1:
                        last.then_inc(sem("conv_done"), 1)
                    else:
                        link(last, 0 if j == CONV - 2 and c == DC - 1 else DC - 1)
            bc = ps[0:96, 0:2, 0:TH]

            def two(ap):
                return ap.rearrange("p (n t) -> p n t", n=2)

            dve.wait_ge(sem("bc_mm"), 2)
            link(V.tensor_copy(two(bcp[:]), bc))
            link(V.tensor_tensor(two(bcr[:]), bc, two(bcp[:]), ALU.subtract))
            V.tensor_copy(bcm[64:96], bcr[64:96])
            link(V.tensor_copy(bcp[32:64], bcr[32:64]))
            V.tensor_tensor(bcp[64:96], bcr[64:96], bcm[64:96], ALU.subtract).then_inc(sem("bc_split"), 1)
            for c in range(DC):
                dve.wait_ge(sem("dt_mm"), 2 * c + 2)
                V.tensor_scalar(two(dtb[:, c, :]), ps[:, 2 + 2 * c:4 + 2 * c, 0:TH], bdt[:, c:c + 1], EXP_SAFE,
                                ALU.add, ALU.min).then_inc(sem("dt_min"), 1)
            for c in range(DC):
                dve.wait_ge(sem("dt_ln"), c + 1)
                V.scalar_tensor_tensor(two(dtb[:, c, :]), ps[:, 2 + 2 * c:4 + 2 * c, 0:TH], bdt[:, c:c + 1],
                                       two(dtb[:, c, :]), ALU.add, ALU.max).then_inc(sem("dt_ready"), 1)
            dve.wait_ge(sem("dt_ready"), DC)
            for c in range(DC):
                last = V.tensor_tensor(dtx[:, c, :], dtb[:, c, :], xc[:, c, :], ALU.mult)
            link(last)

            def scan(u):
                dve.wait_ge(sem("dA_ready"), u + 1)
                dve.wait_ge(sem("dbx_done"), 2 * u + 2)
                if u >= 3:
                    dve.wait_ge(sem("prod_done"), u - 2)
                V.tensor_tensor_scan(hs[:, u % 3].rearrange("p q t -> p (q t)"),
                                     dA[:, u % 3].rearrange("p q t -> p (q t)"),
                                     dBx[:, u % 2].rearrange("p q t -> p (q t)"), 0.0, ALU.mult,
                                     ALU.add).then_inc(sem("scan_done"), 1)

            def skip_and_gate(g):
                c, hf = g // 2, g % 2
                dve.wait_ge(sem("y_mm"), NQ * (g + 1))
                V.scalar_tensor_tensor(half(yz[:, c, :], hf), half(xc[:, c, :], hf), dskip[:, c:c + 1],
                                       ps[:, 6 + g % 2, 0:TH], ALU.mult, ALU.add).then_inc(sem("y_evac"), 1)
                dve.wait_ge(sem("y_evac"), g + 1)
                V.tensor_tensor(half(yz[:, c, :], hf), half(yz[:, c, :], hf), half(zs[:, c, :], hf),
                                ALU.mult).then_inc(sem("yz_ready"), 1)

            for u in range(UNITS + 1):
                if u < UNITS:
                    c, hf = u // (2 * NQ), u // NQ % 2
                    for v in (2 * u, 2 * u + 1):
                        dve.wait_ge(sem("b_mm"), v + 1)
                        if u >= 2 and v % 2 == 0:
                            dve.wait_ge(sem("scan_done"), u - 1)
                        x2 = half(dtx[:, c, :], hf).unsqueeze(1).to_broadcast([P, 2, TH])
                        V.tensor_tensor(dBx[:, u % 2, 2 * (v % 2):2 * (v % 2) + 2],
                                        ps[:, 2 * (v % 2):2 * (v % 2) + 2, 0:TH], x2,
                                        ALU.mult).then_inc(sem("dbx_done"), 1)
                if u >= 1:
                    scan(u - 1)
                if u >= NQ + 3 and (u - 3) % NQ == 0:
                    skip_and_gate((u - 3) // NQ - 1)
            skip_and_gate(2 * DC - 1)
            for i in range(NT):
                dve.wait_ge(sem("mo_mm"), i + 1)
                last = V.tensor_tensor(h[:, i, :], ps[0:TP, i, 0:D], h[:, i, :], ALU.add)
            link(last)

            def experts(L):
                M = hid[L] // P

                def hidden(e, slot):
                    for n in range(2 * M):
                        m, hf = n // 2, n % 2
                        dve.wait_ge(sem(f"gu_mm{L}"), e * (2 * M) + n + 1)
                        if not (isinstance(e, int) and e == 0 and n < 2):
                            dve.wait_ge(sem(f"h_done{L}"), e * (2 * M) + n - 1)
                        if L == 1:
                            V.tensor_scalar(up[:, n % 2, :], ps[:, 2 * (n % 2) + 1, 0:TH], LIMIT, -LIMIT, ALU.min,
                                            ALU.max).then_inc(sem(f"up_done{L}"), 1)
                            dve.wait_ge(sem(f"up_done{L}"), e * (2 * M) + n + 1)
                        dve.wait_ge(sem(f"silu_done{L}"), e * (2 * M) + n + 1)
                        if n == 0 and not (isinstance(e, int) and e < 2):
                            dve.wait_ge(sem(f"down_mm{L}"), (e - 1) * (NT // 2))
                        if L == 1:
                            V.scalar_tensor_tensor(half(hT[:, slot, m, :], hf), gs[:, n % 2, :], SILU_LIMIT,
                                                   up[:, n % 2, :], ALU.min, ALU.mult).then_inc(sem(f"h_done{L}"), 1)
                        else:
                            V.tensor_tensor(half(hT[:, slot, m, :], hf), ps[:, 2 * (n % 2) + 1, 0:TH],
                                            gs[:, n % 2, :], ALU.mult).then_inc(sem(f"h_done{L}"), 1)
                        if n == 3 and not (isinstance(e, int) and e == 0):
                            combine(e - 1)

                def combine(e):
                    if not (isinstance(e, int) and e == 0):
                        dve.wait_ge(sem(f"comb_done{L}"), e * (NT // 2))
                    for b in range(NT // 2):
                        dve.wait_ge(sem(f"down_mm{L}"), e * (NT // 2) + b + 1)
                        for i in (2 * b, 2 * b + 1):
                            src = ps[0:TP, 4 + b, (i % 2) * D:(i % 2 + 1) * D]
                            w = cw[:, e, i:i + 1] if isinstance(e, int) else \
                                cw[:, ds(e, 1), i:i + 1].rearrange("p e i -> p (e i)")
                            if isinstance(e, int) and e == 0 and L == 0:
                                last = V.tensor_scalar(acc[:, i, :], src, w, None, ALU.mult)
                            elif isinstance(e, int) and e == 0:
                                last = V.tensor_tensor(acc[:, i, :], src, h[:, i, :], ALU.add)
                            else:
                                last = V.scalar_tensor_tensor(acc[:, i, :], src, w, acc[:, i, :], ALU.mult, ALU.add)
                        last.then_inc(sem(f"comb_done{L}"), 1)

                hidden(0, 0)
                hidden(1, 1)
                with dve.Fori(1, E // 2) as i:
                    hidden(2 * i, 0)
                    hidden(2 * i + 1, 1)
                if L == 1:
                    hidden(E, 0)
                combine(nexp[L] - 1)
                dve.wait_ge(sem(f"comb_done{L}"), nexp[L] * (NT // 2))

            def bcast(ap):
                return ap.unsqueeze(2).to_broadcast([TP, NT, E])

            def bcast_e(ap):
                return ap.unsqueeze(1).to_broadcast([TP, NT, E])

            def pick(dst, value, top, tmp, best):
                link(V.tensor_tensor(tmp, value, top, ALU.is_ge))
                link(V.tensor_tensor(tmp, tmp, bcast_e(first[:]), ALU.mult))
                link(V.tensor_reduce(best, tmp, AX_X, ALU.max))
                link(V.tensor_tensor(dst, tmp, bcast(best), ALU.is_equal))

            logits = ps[0:TP, 7, 0:NT * E].rearrange("p (n e) -> p n e", n=NT)
            norm(1)
            dve.wait_ge(sem("route_mm0"), 1)
            link(V.tensor_tensor(rt[:, 2], logits, bcast_e(rb[:, 0, :]), ALU.add))
            link(V.tensor_reduce(rs[:, 0], rt[:, 2], AX_X, ALU.max))
            V.tensor_tensor(rt[:, 0], rt[:, 2], bcast(rs[:, 0]), ALU.subtract).then_inc(sem("route_x0"), 1)
            dve.wait_ge(sem("route_exp0"), 1)
            link(V.tensor_reduce(rs[:, 1], rt[:, 1], AX_X, ALU.add))
            link(V.reciprocal(mp[:], rs[:, 1]))
            link(V.tensor_reduce(rs[:, 2], rt[:, 1], AX_X, ALU.max))
            pick(rt[:, 4], rt[:, 1], bcast(rs[:, 2]), rt[:, 3], rs[:, 3])
            link(V.tensor_copy(cw[:, 0:E, :], rt[:, 4].rearrange("p n e -> p e n")))
            experts(0)
            link(V.tensor_copy(accb[:], acc[:]))
            for i in range(NT):
                last = V.scalar_tensor_tensor(h[:, i, :], accb[:, i, :], mp[:, i:i + 1], h[:, i, :], ALU.mult, ALU.add)
            link(last)

            norm(2)
            dve.wait_ge(sem("ld_attn"), 80)
            for n in range(4 * HA):
                m, hf = n // 2, n % 2
                dve.wait_ge(sem("qk_mm"), n + 1)
                if m < HA:
                    V.scalar_tensor_tensor(half(qT[:, m, :], hf), ps[:, 4 + n % 4, 0:TH], DH ** -0.5,
                                           half(qmask, hf), ALU.mult, ALU.add).then_inc(sem("qk_done"), 1)
                else:
                    V.tensor_tensor(half(kT[:, m - HA, :], hf), ps[:, 4 + n % 4, 0:TH], half(kmask, hf),
                                    ALU.add).then_inc(sem("qk_done"), 1)
            dve.wait_ge(sem("attn_consts"), 1)
            for n in range(2 * NG):
                g, jj = n // 2, n % 2
                G = group_tokens(g)
                bank = 2 * (n % 4)
                dve.wait_ge(sem("s_mm"), n + 1)
                for j in range(2):
                    r = 32 * (2 * jj + j) + DH + GI
                    last = V.tensor_reduce(zm[0:G, g, :, r:r + 1],
                                           ps[0:G, bank + j, 0:HA * GT].rearrange("p (a t) -> p a t", a=HA)[:, :, 0:G],
                                           AX_X, ALU.max)
                last.then_inc(sem("max_done"), 1)
            for g in range(NG):
                G = group_tokens(g)
                dve.wait_ge(sem("zm_mm"), g + 1)
                q = qT[:, :, g * GT:g * GT + G]
                V.tensor_tensor(q, ps[:, 6 + g % 2, 0:HA * GT].rearrange("p (a t) -> p a t", a=HA)[:, :, 0:G], q,
                                ALU.add).then_inc(sem("qm_done"), 1)
            for g in range(NG):
                G = group_tokens(g)
                dve.wait_ge(sem("pv_mm"), 2 * g + 2)
                if g >= 2:
                    dve.wait_ge(sem("yT_tr"), g - 1)
                o2 = ps[0:G, 6, 0:NH * (DH + 1)].rearrange("p (h d) -> p h d", h=NH)
                link(V.reciprocal(rden[0:G, g % 2, :].unsqueeze(2), o2[:, :, DH:DH + 1]))
                V.tensor_tensor(yat[0:G, g % 2, :].rearrange("p (h d) -> p h d", h=NH), o2[:, :, 0:DH],
                                rden[0:G, g % 2, :].unsqueeze(2).to_broadcast([G, NH, DH]),
                                ALU.mult).then_inc(sem("yat_done"), 1)
                dve.wait_ge(sem("yT_tr"), g + 1)
                V.tensor_copy(yT[0:KP, :, g * GT:g * GT + G],
                              ps[0:KP, 7, 0:KC * P].rearrange("p (k t) -> p k t", k=KC)[:, :, 0:G]).then_inc(sem("yT_done"), 1)
            for i in range(NT):
                dve.wait_ge(sem("ao_mm"), i + 1)
                last = V.tensor_tensor(h[:, i, :], ps[0:TP, i, 0:D], h[:, i, :], ALU.add)
            link(last)

            norm(3)
            dve.wait_ge(sem("route_mm1"), 1)
            link(V.tensor_copy(rt[:, 6], logits))
            V.tensor_scalar(rt[:, 0], rt[:, 6], EXP_SAFE, None, ALU.min).then_inc(sem("route_x1"), 1)
            dve.wait_ge(sem("route_exp1"), 1)
            link(V.tensor_scalar(rt[:, 2], rt[:, 1], 1.0, None, ALU.add))
            link(V.tensor_scalar(rt[:, 7], rt[:, 2], -1.0, None, ALU.add))
            link(V.tensor_scalar(rt[:, 8], rt[:, 7], 0.0, None, ALU.is_equal))
            V.tensor_tensor(rt[:, 7], rt[:, 7], rt[:, 8], ALU.add).then_inc(sem("route_u1"), 1)
            dve.wait_ge(sem("route_ln1"), 1)
            link(V.tensor_tensor(rt[:, 3], rt[:, 3], rt[:, 8], ALU.add))
            link(V.tensor_tensor(rt[:, 3], rt[:, 3], rt[:, 1], ALU.mult))
            link(V.reciprocal(rt[:, 7], rt[:, 7]))
            link(V.tensor_tensor(rt[:, 3], rt[:, 3], rt[:, 7], ALU.mult))
            V.tensor_tensor(rt[:, 4], rt[:, 3], rt[:, 6], ALU.max).then_inc(sem("route_sp1"), 1)
            dve.wait_ge(sem("route_sqrt1"), 1)
            link(V.tensor_tensor(rt[:, 0], rt[:, 5], bcast_e(rb[:, 1, :]), ALU.add))
            link(V.tensor_reduce(rs[:, 0], rt[:, 0], AX_X, ALU.max))
            pick(rt[:, 9], rt[:, 0], bcast(rs[:, 0]), rt[:, 1], rs[:, 1])
            link(V.scalar_tensor_tensor(rt[:, 0], rt[:, 9], -BIG, rt[:, 0], ALU.mult, ALU.add))
            link(V.tensor_reduce(rs[:, 0], rt[:, 0], AX_X, ALU.max))
            pick(rt[:, 10], rt[:, 0], bcast(rs[:, 0]), rt[:, 1], rs[:, 1])
            link(V.tensor_tensor(rt[:, 9], rt[:, 9], rt[:, 10], ALU.add))
            link(V.tensor_tensor(rt[:, 9], rt[:, 9], rt[:, 5], ALU.mult))
            link(V.tensor_reduce(rs[:, 2], rt[:, 9], AX_X, ALU.add))
            link(V.tensor_scalar(rs[:, 2], rs[:, 2], 1e-6, None, ALU.max))
            link(V.reciprocal(rs[:, 3], rs[:, 2]))
            link(V.tensor_tensor(cw[:, 1:E + 1, :], rt[:, 9].rearrange("p n e -> p e n"),
                                 rs[:, 3].unsqueeze(1).to_broadcast([TP, E, NT]), ALU.mult))
            experts(1)
            for i in range(NT):
                V.tensor_copy(h[:, i, :], acc[:, i, :]).then_inc(sem("h_final"), 1)


def kernel(**inputs):
    import numpy as _np
    import concourse.bacc as _bacc
    from concourse import mybir as _mybir
    from concourse.bass_utils import run_bass_kernel_spmd as _run
    import ml_dtypes as _ml

    f = {k: _np.asarray(v) for k, v in inputs.items()}

    def rows(w, p):
        return w.reshape(w.shape[0] // p, p, w.shape[1]).transpose(1, 0, 2)

    def col(v):
        return v.reshape(-1, P).T

    def every(v):
        return _np.broadcast_to(v, (TP,) + v.shape)

    patches = f["x"].reshape(B, CH, SIDE, PATCH, SIDE, PATCH).transpose(0, 2, 4, 3, 5, 1).reshape(T, PD)
    sel = _np.zeros((96, 32, P), _ml.bfloat16)
    sel[_np.arange(96), _np.arange(96) % 32, :] = 1
    qmask = _np.zeros((P, T), _np.float32)
    kmask = _np.zeros((P, T), _np.float32)
    img = _np.arange(T) // S % GI
    for j in range(HG):
        for r in range(GI):
            qmask[32 * j + DH + r] = img == r
            kmask[32 * j + DH + r] = _np.where(img == r, 0.0, -BIG)
        kmask[32 * j + DH + GI] = -1.0
    wbc = _np.concatenate([f["L0_attn_W_B"], f["L0_attn_W_C"]], 0)
    wqkv = f["L1_attn_w_qkv"]
    wqk = _np.zeros((D, 2, HA, HG, 32), _np.float32)
    wqk[..., 0:DH] = wqkv[:, 0:2 * D].reshape(D, 2, HA, HG, DH)
    gu0 = _np.concatenate([f["L0_ffn_w1"], f["L0_ffn_w2"]], 2)
    w1 = _np.concatenate([f["L1_ffn_w1s"][None], f["L1_ffn_w1"]], 0)
    w3 = _np.concatenate([f["L1_ffn_w3s"][None], f["L1_ffn_w3"]], 0)
    w2 = _np.concatenate([f["L1_ffn_w2s"][None], f["L1_ffn_w2"]], 0)
    gu1 = _np.concatenate([w1, w3], 2)
    dn0 = f["L0_ffn_w3"]

    def experts(w, p):
        return w.reshape(w.shape[0], w.shape[1] // p, p, w.shape[2]).transpose(0, 2, 1, 3)

    arrays = {
        "wp": rows(f["L0_tok_W_proj"].T, P), "gin": col(f["L0_tok_g_in"]),
        "xT": rows(patches.T, P), "xtok": rows(patches, TP),
        "bproj": every(f["L0_tok_b_proj"]), "gout": every(f["L0_tok_g_out"]),
        "ident": _np.eye(P, dtype=_np.float32),
        "win": rows(f["L0_attn_W_in"].T, KP),
        "wconv": f["L0_attn_W_conv"].reshape(DC, P, CONV).transpose(1, 0, 2), "bconv": col(f["L0_attn_b_conv"]),
        "wdt": rows(f["L0_attn_W_dt"].T, P), "bdt": col(f["L0_attn_b_dt"]),
        "alog": f["L0_attn_A_log"].reshape(DC, P, NS).transpose(1, 0, 2), "dskip": col(f["L0_attn_D_skip"]),
        "wbc": rows(_np.concatenate([wbc, wbc, wbc], 0).T, P), "sel": sel,
        "wout": rows(f["L0_attn_W_out"].T, P),
        "wr": _np.stack([rows(f["L0_ffn_router_w"], KP), rows(f["L1_ffn_gate_w"], KP)], 1),
        "rb": every(_np.stack([f["L0_ffn_router_b"], f["L1_ffn_gate_bias"]], 0)),
        "first": every(_np.arange(E, 0, -1).astype(_np.float32)),
        "wqk": rows(wqk.reshape(D, -1), KP), "wv": rows(wqkv[:, 2 * D:], KP), "wpr": rows(f["L1_attn_w_proj"], KP),
        "qmask": qmask, "kmask": kmask,
        "gu0": experts(gu0, KP), "dn0": experts(dn0, P), "gu1": experts(gu1, KP), "dn1": experts(w2, P),
    }
    nc = _bacc.Bacc("TRN2", target_bir_lowering=False, num_devices=1)
    arrays = {f"in_{k}": _np.ascontiguousarray(v) for k, v in arrays.items()}
    args = {k[3:]: nc.dram_tensor(k, v.shape, _mybir.dt.from_np(v.dtype), kind="ExternalInput").ap()
            for k, v in arrays.items()}
    out = nc.dram_tensor("out_0", (T, D), _mybir.dt.float32, kind="ExternalOutput").ap()
    build(nc, args, out)
    r = _run(nc, [arrays], core_ids=[0])
    return r.results[0]["out_0"].reshape(B, S, D)
```
